# Optimizing a Trainium2 kernel written in Bass

```python
import numpy as np
import jax
import jax.numpy as jnp

def _softmax(x, axis=-1):
    return jax.nn.softmax(x, axis=axis)

def _gelu(x):
    return jax.nn.gelu(x, approximate=True)

def _silu(x):
    return jax.nn.silu(x)

def _sigmoid(x):
    return jax.nn.sigmoid(x)

def _layernorm(x, axis=-1, eps=1e-05):
    m = jnp.mean(x, axis=axis, keepdims=True)
    v = jnp.var(x, axis=axis, keepdims=True)
    return (x - m) / jnp.sqrt(v + eps)

def _scatter_add(tgt, idx, src, axis=0):
    return tgt.at[idx].add(src)

def _segment_sum(src, seg, n):
    return jax.ops.segment_sum(src, seg, n)
kernel_name = 'mk_cond_seq_d2_seqx_r4_bb86fc'

def setup_inputs(seed: int=0):
    np.random.seed(seed)
    _w = jnp.asarray

    def _rec_inputs():
        import jax
        import jax.numpy as jnp
        _rk = jax.random.key(seed)
        x = -0.0003929 + 0.9999 * jax.random.normal(jax.random.fold_in(_rk, 1), (128, 64, 256), jnp.float32)
        _lenS = 64 - jax.random.randint(jax.random.fold_in(_rk, 7), (128,), 0, max(1, 64 // 4) + 1, jnp.int32)
        _lenS2 = 64 - jax.random.randint(jax.random.fold_in(_rk, 8), (128,), 0, max(1, 64 // 4) + 1, jnp.int32)
        cond_2048 = 0.00782532 + 1.00527 * jax.random.normal(jax.random.fold_in(_rk, 11), (128, 512), jnp.float32)
        itok_S_0_1023 = jax.random.randint(jax.random.fold_in(_rk, 13), (64,), 0, 256, jnp.int32)
        _validS = jnp.arange(64)[None, :] < _lenS[:, None]
        _validS2 = jnp.arange(64)[None, :] < _lenS2[:, None]
        _causal = jnp.tril(jnp.ones((64, 64), dtype=bool))
        mask_BxS_ik0 = jnp.where(jnp.broadcast_to(_validS[:, :], (128, 64)), 0, 1).astype(jnp.int32)
        return (x, cond_2048, itok_S_0_1023, mask_BxS_ik0)
    x, cond_2048, itok_S_0_1023, mask_BxS_ik0 = _rec_inputs()

    def _L0_cond_setup():
        import jax, jax.numpy as jnp
        import numpy as np
        H = 16
        LN_EPS = 1e-05

        def _layernorm(x, scale, bias):
            mu = jnp.mean(x, axis=-1, keepdims=True)
            var = jnp.var(x, axis=-1, keepdims=True)
            return (x - mu) * jax.lax.rsqrt(var + LN_EPS) * scale + bias
        key = jax.random.key(seed)
        ks = jax.random.split(key, 8)
        B, T, D, E = (4, 1024, 256, 512)
        s = 0.02
        return {'x': jax.random.normal(ks[0], (B, T, D), jnp.float32), 'emb': jax.random.normal(ks[1], (B, E), jnp.float32), 'src_mask': jax.random.randint(ks[2], (B, T), 0, 2).astype(jnp.int32), 'norm_scale': jnp.ones((D,), jnp.float32), 'norm_bias': jnp.zeros((D,), jnp.float32), 'Wq': jax.random.normal(ks[3], (D, D), jnp.float32) * s, 'bq': jnp.zeros((D,), jnp.float32), 'Wk': jax.random.normal(ks[4], (D, D), jnp.float32) * s, 'bk': jnp.zeros((D,), jnp.float32), 'Wv': jax.random.normal(ks[5], (D, D), jnp.float32) * s, 'bv': jnp.zeros((D,), jnp.float32), 'film_emb_W': jax.random.normal(ks[6], (E, 2 * D), jnp.float32) * s, 'film_emb_b': jnp.zeros((2 * D,), jnp.float32), 'film_norm_scale': jnp.ones((D,), jnp.float32), 'film_norm_bias': jnp.zeros((D,), jnp.float32), 'film_out_W': jax.random.normal(ks[7], (D, D), jnp.float32) * s, 'film_out_b': jnp.zeros((D,), jnp.float32)}
    _L0_cond_all = _L0_cond_setup()
    _L0_cond_in = {k: v for k, v in _L0_cond_all.items() if k in ('norm_scale', 'norm_bias', 'Wq', 'bq', 'Wk', 'bk', 'Wv', 'bv', 'film_emb_W', 'film_emb_b', 'film_norm_scale', 'film_norm_bias', 'film_out_W', 'film_out_b')}
    del _L0_cond_all

    def _L1_cond_setup():
        import jax, jax.numpy as jnp
        import numpy as np
        B_SZ, S, D = (4, 256, 256)
        DI, DS, DTR, DC = (512, 16, 64, 4)
        EPS = 1e-05

        def _layernorm(x, g, b):
            m = jnp.mean(x, axis=-1, keepdims=True)
            v = jnp.var(x, axis=-1, keepdims=True)
            return (x - m) * jax.lax.rsqrt(v + EPS) * g + b

        def _mamba(h, W_in, conv_w, conv_b, W_xp, W_dt, b_dt, A_log, D_param, W_out):
            bsz = h.shape[0]
            xz = h @ W_in
            xm, z = jnp.split(xz, 2, axis=-1)
            xc = jnp.transpose(xm, (0, 2, 1))
            xc = jax.lax.conv_general_dilated(xc, conv_w, (1,), [(DC - 1, 0)], feature_group_count=DI, dimension_numbers=('NCH', 'OIH', 'NCH'))
            xc = xc + conv_b[None, :, None]
            xm = jax.nn.silu(jnp.transpose(xc, (0, 2, 1)))
            xdbl = xm @ W_xp
            dtr, Bm, Cm = jnp.split(xdbl, [DTR, DTR + DS], axis=-1)
            dt = jax.nn.softplus(dtr @ W_dt + b_dt)
            A = -jnp.exp(A_log)

            def step(hst, inp):
                dt_t, B_t, C_t, x_t = inp
                dA = jnp.exp(dt_t[:, :, None] * A)
                hst = hst * dA + (dt_t * x_t)[:, :, None] * B_t[:, None, :]
                y = jnp.einsum('bds,bs->bd', hst, C_t)
                return (hst, y)
            inputs = (jnp.transpose(dt, (1, 0, 2)), jnp.transpose(Bm, (1, 0, 2)), jnp.transpose(Cm, (1, 0, 2)), jnp.transpose(xm, (1, 0, 2)))
            h0 = jnp.zeros((bsz, DI, DS), dt.dtype)
            _, ys = jax.lax.scan(step, h0, inputs)
            y = jnp.transpose(ys, (1, 0, 2)) + xm * D_param
            y = y * jax.nn.silu(z)
            return y @ W_out
        key = jax.random.key(seed)
        ks = jax.random.split(key, 12)

        def w(k, shape, scale=0.02):
            return jax.random.normal(k, shape, jnp.float32) * scale
        x = jax.random.normal(ks[0], (B_SZ, S, D), jnp.float32)
        c = jax.random.normal(ks[1], (B_SZ, 2 * D), jnp.float32)
        W_ada = w(ks[2], (2 * D, 3 * D))
        b_ada = jnp.zeros((3 * D,), jnp.float32)
        gamma = jnp.ones((D,), jnp.float32)
        beta = jnp.zeros((D,), jnp.float32)
        W_in = w(ks[3], (D, 2 * DI))
        conv_w = w(ks[4], (DI, 1, DC), 0.1)
        conv_b = jnp.zeros((DI,), jnp.float32)
        W_xp = w(ks[5], (DI, DTR + 2 * DS))
        W_dt = w(ks[6], (DTR, DI))
        b_dt = jnp.full((DI,), jnp.log(jnp.expm1(jnp.float32(0.01))), jnp.float32)
        A_log = jnp.log(jnp.broadcast_to(jnp.arange(1, DS + 1, dtype=jnp.float32), (DI, DS)))
        D_param = jnp.ones((DI,), jnp.float32)
        W_out = w(ks[7], (DI, D))
        perm = jax.random.permutation(ks[8], S)
        inv_perm = jnp.argsort(perm)
        return dict(x=x, c=c, W_ada=W_ada, b_ada=b_ada, gamma=gamma, beta=beta, W_in=W_in, conv_w=conv_w, conv_b=conv_b, W_xp=W_xp, W_dt=W_dt, b_dt=b_dt, A_log=A_log, D_param=D_param, W_out=W_out, perm=perm, inv_perm=inv_perm)
    _L1_cond_all = _L1_cond_setup()
    _L1_cond_in = {k: v for k, v in _L1_cond_all.items() if k in ('W_ada', 'b_ada', 'gamma', 'beta', 'W_in', 'conv_w', 'conv_b', 'W_xp', 'W_dt', 'b_dt', 'A_log', 'D_param', 'W_out')}
    del _L1_cond_all
    return {'x': x, 'cond_2048': cond_2048, 'itok_S_0_1023': itok_S_0_1023, 'mask_BxS_ik0': mask_BxS_ik0, 'L0_cond_norm_scale': _L0_cond_in['norm_scale'], 'L0_cond_norm_bias': _L0_cond_in['norm_bias'], 'L0_cond_Wq': _L0_cond_in['Wq'], 'L0_cond_bq': _L0_cond_in['bq'], 'L0_cond_Wk': _L0_cond_in['Wk'], 'L0_cond_bk': _L0_cond_in['bk'], 'L0_cond_Wv': _L0_cond_in['Wv'], 'L0_cond_bv': _L0_cond_in['bv'], 'L0_cond_film_emb_W': _L0_cond_in['film_emb_W'], 'L0_cond_film_emb_b': _L0_cond_in['film_emb_b'], 'L0_cond_film_norm_scale': _L0_cond_in['film_norm_scale'], 'L0_cond_film_norm_bias': _L0_cond_in['film_norm_bias'], 'L0_cond_film_out_W': _L0_cond_in['film_out_W'], 'L0_cond_film_out_b': _L0_cond_in['film_out_b'], 'L1_cond_W_ada': _L1_cond_in['W_ada'], 'L1_cond_b_ada': _L1_cond_in['b_ada'], 'L1_cond_gamma': _L1_cond_in['gamma'], 'L1_cond_beta': _L1_cond_in['beta'], 'L1_cond_W_in': _L1_cond_in['W_in'], 'L1_cond_conv_w': _L1_cond_in['conv_w'], 'L1_cond_conv_b': _L1_cond_in['conv_b'], 'L1_cond_W_xp': _L1_cond_in['W_xp'], 'L1_cond_W_dt': _L1_cond_in['W_dt'], 'L1_cond_b_dt': _L1_cond_in['b_dt'], 'L1_cond_A_log': _L1_cond_in['A_log'], 'L1_cond_D_param': _L1_cond_in['D_param'], 'L1_cond_W_out': _L1_cond_in['W_out']}

def reference(x, cond_2048, itok_S_0_1023, mask_BxS_ik0, L0_cond_norm_scale, L0_cond_norm_bias, L0_cond_Wq, L0_cond_bq, L0_cond_Wk, L0_cond_bk, L0_cond_Wv, L0_cond_bv, L0_cond_film_emb_W, L0_cond_film_emb_b, L0_cond_film_norm_scale, L0_cond_film_norm_bias, L0_cond_film_out_W, L0_cond_film_out_b, L1_cond_W_ada, L1_cond_b_ada, L1_cond_gamma, L1_cond_beta, L1_cond_W_in, L1_cond_conv_w, L1_cond_conv_b, L1_cond_W_xp, L1_cond_W_dt, L1_cond_b_dt, L1_cond_A_log, L1_cond_D_param, L1_cond_W_out):
    import jax
    import jax.numpy as jnp

    def _L0_cond_ref(x, emb, src_mask, norm_scale, norm_bias, Wq, bq, Wk, bk, Wv, bv, film_emb_W, film_emb_b, film_norm_scale, film_norm_bias, film_out_W, film_out_b):
        import jax, jax.numpy as jnp
        import numpy as np
        H = 16
        LN_EPS = 1e-05

        def _layernorm(x, scale, bias):
            mu = jnp.mean(x, axis=-1, keepdims=True)
            var = jnp.var(x, axis=-1, keepdims=True)
            return (x - mu) * jax.lax.rsqrt(var + LN_EPS) * scale + bias
        B, T, D = x.shape
        dh = D // H
        xn = _layernorm(x, norm_scale, norm_bias)
        q = xn @ Wq + bq
        k = xn @ Wk + bk
        v = xn @ Wv + bv
        mask = (src_mask == 1)[:, :, None]
        k = jnp.where(mask, -jnp.inf, k)
        v = jnp.where(mask, 0.0, v)
        q = q.reshape(B, T, H, dh).transpose(0, 2, 1, 3)
        k = k.reshape(B, T, H, dh).transpose(0, 2, 1, 3)
        v = v.reshape(B, T, H, dh).transpose(0, 2, 1, 3)
        q = jax.nn.softmax(q, axis=-1)
        k = jax.nn.softmax(k, axis=2)
        attn = jnp.einsum('bhse,bhsd->bhed', k, v)
        y = jnp.einsum('bhtd,bhed->bhte', q, attn)
        y = y.transpose(0, 2, 1, 3).reshape(B, T, D)
        emb_out = jax.nn.silu(emb) @ film_emb_W + film_emb_b
        scale, shift = jnp.split(emb_out, 2, axis=-1)
        h = _layernorm(y, film_norm_scale, film_norm_bias) * (1.0 + scale[:, None, :]) + shift[:, None, :]
        h = jax.nn.silu(h) @ film_out_W + film_out_b
        return x + h

    def _L1_cond_ref(x, c, W_ada, b_ada, gamma, beta, W_in, conv_w, conv_b, W_xp, W_dt, b_dt, A_log, D_param, W_out, perm, inv_perm):
        import jax, jax.numpy as jnp
        import numpy as np
        B_SZ, S, D = (4, 256, 256)
        DI, DS, DTR, DC = (512, 16, 64, 4)
        EPS = 1e-05

        def _layernorm(x, g, b):
            m = jnp.mean(x, axis=-1, keepdims=True)
            v = jnp.var(x, axis=-1, keepdims=True)
            return (x - m) * jax.lax.rsqrt(v + EPS) * g + b

        def _mamba(h, W_in, conv_w, conv_b, W_xp, W_dt, b_dt, A_log, D_param, W_out):
            bsz = h.shape[0]
            xz = h @ W_in
            xm, z = jnp.split(xz, 2, axis=-1)
            xc = jnp.transpose(xm, (0, 2, 1))
            xc = jax.lax.conv_general_dilated(xc, conv_w, (1,), [(DC - 1, 0)], feature_group_count=DI, dimension_numbers=('NCH', 'OIH', 'NCH'))
            xc = xc + conv_b[None, :, None]
            xm = jax.nn.silu(jnp.transpose(xc, (0, 2, 1)))
            xdbl = xm @ W_xp
            dtr, Bm, Cm = jnp.split(xdbl, [DTR, DTR + DS], axis=-1)
            dt = jax.nn.softplus(dtr @ W_dt + b_dt)
            A = -jnp.exp(A_log)

            def step(hst, inp):
                dt_t, B_t, C_t, x_t = inp
                dA = jnp.exp(dt_t[:, :, None] * A)
                hst = hst * dA + (dt_t * x_t)[:, :, None] * B_t[:, None, :]
                y = jnp.einsum('bds,bs->bd', hst, C_t)
                return (hst, y)
            inputs = (jnp.transpose(dt, (1, 0, 2)), jnp.transpose(Bm, (1, 0, 2)), jnp.transpose(Cm, (1, 0, 2)), jnp.transpose(xm, (1, 0, 2)))
            h0 = jnp.zeros((bsz, DI, DS), dt.dtype)
            _, ys = jax.lax.scan(step, h0, inputs)
            y = jnp.transpose(ys, (1, 0, 2)) + xm * D_param
            y = y * jax.nn.silu(z)
            return y @ W_out
        mod = jax.nn.silu(c) @ W_ada + b_ada
        shift, scale, gate = jnp.split(mod, 3, axis=1)
        h = _layernorm(x, gamma, beta)
        h = h * (1.0 + scale[:, None, :]) + shift[:, None, :]
        h = h[:, perm]
        y = _mamba(h, W_in, conv_w, conv_b, W_xp, W_dt, b_dt, A_log, D_param, W_out)
        y = y[:, inv_perm]
        return x + gate[:, None, :] * y
    x = _L0_cond_ref(x, cond_2048, mask_BxS_ik0, L0_cond_norm_scale, L0_cond_norm_bias, L0_cond_Wq, L0_cond_bq, L0_cond_Wk, L0_cond_bk, L0_cond_Wv, L0_cond_bv, L0_cond_film_emb_W, L0_cond_film_emb_b, L0_cond_film_norm_scale, L0_cond_film_norm_bias, L0_cond_film_out_W, L0_cond_film_out_b)
    x = _L1_cond_ref(x, cond_2048, L1_cond_W_ada, L1_cond_b_ada, L1_cond_gamma, L1_cond_beta, L1_cond_W_in, L1_cond_conv_w, L1_cond_conv_b, L1_cond_W_xp, L1_cond_W_dt, L1_cond_b_dt, L1_cond_A_log, L1_cond_D_param, L1_cond_W_out, itok_S_0_1023, itok_S_0_1023)
    return x

_drawn_inputs = setup_inputs


def setup_inputs(seed=0):
    import zlib

    import numpy as np

    out = dict(_drawn_inputs(seed))
    spreads = {'L0_cond_norm_scale': (1.0, 0.2),
     'L0_cond_norm_bias': (0.0, 0.1),
     'L0_cond_bq': (0.0, 0.1),
     'L0_cond_bk': (0.0, 0.1),
     'L0_cond_bv': (0.0, 0.1),
     'L0_cond_film_emb_b': (0.0, 0.1),
     'L0_cond_film_norm_scale': (1.0, 0.2),
     'L0_cond_film_norm_bias': (0.0, 0.1),
     'L0_cond_film_out_b': (0.0, 0.1),
     'L1_cond_b_ada': (0.0, 0.1),
     'L1_cond_gamma': (1.0, 0.2),
     'L1_cond_beta': (0.0, 0.1),
     'L1_cond_conv_b': (0.0, 0.1),
     'L1_cond_b_dt': (-4.600166320800781, 0.2),
     'L1_cond_D_param': (1.0, 0.2)}
    factors = {}
    for name, (base, spread) in spreads.items():
        noise = np.random.default_rng([zlib.crc32(name.encode()), seed]).standard_normal(out[name].shape)
        drawn = base * np.exp(spread * noise) if base else spread * noise
        out[name] = jnp.asarray(drawn.astype(out[name].dtype))
    for name, factor in factors.items():
        out[name] = (out[name] * factor).astype(out[name].dtype)
    return out
```

```python
from contextlib import ExitStack

import concourse.bass as bass
from concourse import mybir

ALU = mybir.AluOpType
ACT = mybir.ActivationFunctionType
AX = mybir.AxisListType
F32 = mybir.dt.float32
I32 = mybir.dt.int32

P = 128
BATCH, STEPS, D = 128, 64, 256
COND = 512
HEADS = 16
DH = D // HEADS
FB = D // P
TILES = BATCH * STEPS // P
SEQS = P // STEPS
DI, DS, DTR, TAPS = 512, 16, 64, 4
CB = DI // P
KC = COND // P
T = 4
CHUNKS = STEPS // T
TOK = T * P
ITEMS = DS * T
PAIR = 2 * T
DECAY_BANKS = 3
ON_VECTOR = (2, 5, 8, 11)
EPS = 1e-5
XRING = 4


def build(nc, x, cond, itok, mask, norm_scale, norm_bias, Wq, bq, Wk, bk, Wv, bv,
          film_W, film_b, film_norm_scale, film_norm_bias, film_out_W, film_out_b,
          W_ada, b_ada, gamma, beta, W_in, conv_w, conv_b, W_xp, W_dt, b_dt, A_log, D_param, W_out, out):
    x_tok = x.rearrange("b t f -> (b t) f")
    mask_flat = mask.rearrange("b t -> (b t)")
    resid = nc.dram_tensor("resid", (BATCH * STEPS, D), F32, kind="Internal").ap()
    normed = nc.dram_tensor("normed", (BATCH * STEPS, D), F32, kind="Internal").ap()
    ssm_out = nc.dram_tensor("ssm_out", (BATCH, STEPS, D), F32, kind="Internal").ap()
    resid_seq = resid.rearrange("(b t) f -> b t f", t=STEPS)
    normed_seq = normed.rearrange("(b t) f -> b t f", t=STEPS)

    with ExitStack() as ctx:
        def sem(name):
            return ctx.enter_context(nc.semaphore(name))

        def sb(name, shape, stack=ctx, dt=F32):
            return stack.enter_context(nc.sbuf_tensor(name, shape, dt))

        ident = sb("ident", [P, P])
        ones_row = sb("ones_row", [1, P])
        order = sb("order", [1, STEPS], dt=I32)
        w_in = sb("w_in", [P, FB, 2 * DI])
        w_xp = sb("w_xp", [P, CB, DTR + 2 * DS])
        w_dt = sb("w_dt", [DTR, DI])
        w_out = sb("w_out", [P, CB, D])
        d_diag = sb("d_diag", [P, CB, P])
        decay_rate = sb("decay_rate", [P, CB, DS])
        taps = sb("taps", [P, CB, TAPS])
        col = sb("col", [P, 32])
        conv_bias, dt_bias, d_col = (col[:, 4 * i:4 * i + 4] for i in range(3))
        ns_col, nb_col, bk_col, fns_col, fnb_col = (col[:, 12 + 2 * i:14 + 2 * i] for i in range(5))
        fb_col = col[:, 22:26]
        mod_scale = sb("mod_scale", [P, D])
        mod_shift = sb("mod_shift", [P, D])
        mod_gate = sb("mod_gate", [P, D])

        attn_mem = ExitStack()
        xt = sb("xt", [P, XRING, D], attn_mem)
        w_qv = sb("w_qv", [P, FB, 2 * D], attn_mem)
        w_k = sb("w_k", [P, FB, D], attn_mem)
        w_fo = sb("w_fo", [P, FB, D], attn_mem)
        b_qv = sb("b_qv", [1, 2 * D], attn_mem)
        b_fo = sb("b_fo", [1, D], attn_mem)
        b_mod = sb("b_mod", [1, 3 * D], attn_mem)
        film_w = sb("film_w", [P, KC, 2 * D], attn_mem)
        ada_w = sb("ada_w", [P, KC, 3 * D], attn_mem)
        cond_s = sb("cond_s", [P, COND], attn_mem)
        cond_t = sb("cond_t", [P, COND], attn_mem)
        cond_T = sb("cond_T", [P, KC, P], attn_mem)
        gamma_bc = sb("gamma_bc", [P, D], attn_mem)
        beta_bc = sb("beta_bc", [P, D], attn_mem)
        film_s = sb("film_s", [P, FB, P], attn_mem)
        film_t = sb("film_t", [P, FB, P], attn_mem)
        head_mask = sb("head_mask", [P, 4, P], attn_mem)
        mask_i = sb("mask_i", [STEPS, P], attn_mem, I32)
        mask_f = sb("mask_f", [STEPS, P], attn_mem)
        keep = sb("keep", [P, TILES], attn_mem)
        order_i = sb("order_i", [1, STEPS], attn_mem, I32)
        order_f = sb("order_f", [1, 2, STEPS], attn_mem)
        mask_bc = sb("mask_bc", [P, 2, P], attn_mem, I32)
        mneg = sb("mneg", [P, 2, P], attn_mem)
        half_pow = sb("half_pow", [P, 1], attn_mem)
        stats = sb("stats", [P, 3, 6], attn_mem)
        mv = sb("mv", [P, 3, 2, 2], attn_mem)
        rstd = sb("rstd", [P, 3, 2, 2], attn_mem)
        xn = sb("xn", [P, D], attn_mem)
        xnT = sb("xnT", [P, 2, FB, P], attn_mem)
        qmax = sb("qmax", [P, HEADS], attn_mem)
        qe = sb("qe", [P, 2, D], attn_mem)
        qsum = sb("qsum", [P, HEADS], attn_mem)
        qrec = sb("qrec", [P, 4, HEADS], attn_mem)
        vt = sb("vt", [P, 2, D], attn_mem)
        kT = sb("kT", [P, 2, FB * SEQS, STEPS], attn_mem)
        kmax = sb("kmax", [P, FB * SEQS], attn_mem)
        ksum = sb("ksum", [P, FB * SEQS], attn_mem)
        krec = sb("krec", [P, FB * SEQS], attn_mem)
        kq = sb("kq", [P, 2, 2 * D], attn_mem)
        attnT = sb("attnT", [P, 4, P], attn_mem)
        yt = sb("yt", [P, D], attn_mem)
        yn = sb("yn", [P, D], attn_mem)
        fu = sb("fu", [P, D], attn_mem)
        fth = sb("fth", [P, D], attn_mem)
        fs = sb("fs", [P, FB, P], attn_mem)
        x1 = sb("x1", [P, 2, D], attn_mem)
        xh = sb("xh", [P, 2, D], attn_mem)
        attn_mem.close()

        ssm_mem = ExitStack()
        xg = sb("xg", [P, T, D], ssm_mem)
        hT = sb("hT", [P, FB, TOK], ssm_mem)
        raw = sb("raw", [P, CB, (TAPS - 1) * P + TOK], ssm_mem)
        xs = sb("xs", [P, CB, TOK], ssm_mem)
        tmp = sb("tmp", [P, CB, TOK], ssm_mem)
        dtrT = sb("dtrT", [DTR, TOK], ssm_mem)
        bc = sb("bc", [P, 2, T, 2 * DS], ssm_mem)
        dtT = sb("dtT", [P, 2, CB, TOK], ssm_mem)
        dtx = sb("dtx", [P, 2, T, DI], ssm_mem)
        zs = sb("zs", [P, T, DI], ssm_mem)
        decay = sb("decay", [P, 4, CB, TOK], ssm_mem)
        c_diag = sb("c_diag", [P, 4, T, P], ssm_mem)
        state = sb("state", [P, DS, DI], ssm_mem)
        fresh = sb("fresh", [P, 2, 2, DI], ssm_mem)
        gT = sb("gT", [P, 2, CB, P], ssm_mem)
        part = sb("part", [P, T, DI], ssm_mem)
        yo = sb("yo", [P, 2, 2, D], ssm_mem)
        ssm_mem.close()
        end_mem = ExitStack()
        fin_r = sb("fin_r", [P, 2, 8, D], end_mem)
        fin_y = sb("fin_y", [P, 2, 8, D], end_mem)
        end_mem.close()

        bank = [ctx.enter_context(nc.psum_tensor(f"bank{i}", [P, 512], F32)) for i in range(8)]
        b_xT, b_qvp, b_kT, b_kq, b_at, b_y, b_ynT, b_fo_ps = bank
        y_bank = bank[0:4]
        dec_bank = bank[4:7]
        side = bank[7]

        s_x = [sem(f"x_loaded{i}") for i in range(XRING)]
        s_mk = [sem(f"mask_row_loaded{i}") for i in range(2)]
        s_cols = sem("columns_loaded")
        s_attn_w = sem("attention_weights_loaded")
        s_cond = sem("conditioning_loaded")
        s_ssm_w = sem("mamba_weights_loaded")
        s_pool = sem("pool_constants")
        s_const = sem("constants_done")
        s_ve = sem("vector_setup")
        s_ae = sem("scalar_setup")
        s_pe = sem("tensor_setup")
        s_step = sem("vector_setup_steps")
        s_apart = sem("waits_apart")
        names = ("x_stats x_meanvar x_rstd x_norm xT_ready xnT_ready qv_ready kT_ready mneg_ready "
                 "k_biased k_max k_shifted k_exp k_sum k_rec k_normed q_max q_shifted q_exp q_sum q_rec v_ready "
                 "kq_turned kq_ready at_half at_ready at_masked y_ready y_scaled y_stats y_meanvar y_rstd y_norm ynT_ready "
                 "film_in film_tanh film_act proj_ready x1_ready x1_stats x1_meanvar x1_rstd xh_ready "
                 "x_plus y_plus x1_plus").split()
        S = {n: sem(n) for n in names}
        s_x1_out = [sem(f"x1_stored{i}") for i in range(2)]
        s_xh_out = [sem(f"xh_stored{i}") for i in range(2)]

        block = ctx.enter_context(nc.Block())

        def apart(eng):
            eng.sem_inc(s_apart, 1)

        def later(eng, s, tile, need=1):
            eng.wait_ge(s, tile + need)

        def reuse(eng, s, tile, slots):
            if not isinstance(tile, int) or tile >= slots:
                eng.wait_ge(s, tile + (1 - slots))

        def attention_iterations(eng, iteration):
            for j in range(4):
                iteration(j, j, [s for s in range(5) if j - s >= 0])
            with eng.Fori(4, TILES - 3, 4) as j0:
                for u in range(4):
                    iteration(j0 + u, u, [0, 1, 2, 3, 4])
            for j in range(TILES, TILES + 4):
                iteration(j, j % 4, [s for s in range(5) if j - s < TILES])

        s_xg = sem("rows_gathered")
        s_side_filled = sem("side_filled")
        s_side_moved = sem("side_moved")
        s_modulated = sem("modulated")
        s_carried = sem("conv_carry_copied")
        s_tap = sem("conv_taps_added")
        s_tap0 = sem("conv_first_tap")
        s_xtanh, s_xs = sem("x_tanh"), sem("xs_ready")
        s_ztanh, s_zs = sem("z_tanh"), sem("zs_ready")
        s_softexp, s_dt = sem("softplus_steps"), sem("dt_ready")
        s_dtxT = sem("dt_times_x")
        s_decay = sem("decay_ready")
        s_turned = sem("decay_turned")
        s_kept = sem("state_decayed")
        s_state = sem("state_updated")
        s_read = sem("state_read_out")
        s_part = sem("state_read_by_vector")
        s_cdiag = sem("c_diag_ready")
        s_skip = sem("skip_term_added")
        s_gated = sem("y_gated")
        s_summed = sem("y_shares_summed")
        s_yo = sem("y_rows_ready")
        s_y_out = [sem(f"y_rows_stored{i}") for i in range(2)]
        s_prep = sem("mamba_constants")
        s_prep_a = sem("mamba_constants_scalar")
        s_fin_r = [sem(f"final_resid_loaded{i}") for i in range(2)]
        s_fin_y = [sem(f"final_y_loaded{i}") for i in range(2)]
        s_sum = sem("final_sum")
        s_out = sem("out_stored")

        JOBS = ("turn0 turn1 out0 turn2 turn3 out1 z0 z1 z2 z3 "
                "h0 h1 u0 u1 u2 u3 dtr dt0 dt1 dt2 dt3 bc x0 x1 x2 x3").split()
        POSTS, ZS = 6, 4
        SLOTS = dict(zip(JOBS, ((1,), (2,), (3, 4, 5), (8,), (9,), (10, 11, 12), (15, 16), (17, 18), (19, 20), (21, 22),
                                (23,), (24,), (25, 26), (27, 28), (29, 30), (31, 32), (43, 44, 45, 46),
                                (48,), (49,), (50,), (51,), (52, 53, 54, 55), (60,), (61,), (62,), (63,))))
        TAP_SLOT = 28
        TAP_ORDER = [(m, w - m) for w in range(CB + TAPS - 2) for m in range(CB) if 0 <= w - m < TAPS - 1]

        def product(c, job):
            n = JOBS.index(job)
            if isinstance(c, int) and c == -1:
                return n - POSTS - ZS
            if isinstance(c, int) and c == CHUNKS:
                return len(JOBS) * (CHUNKS - 1) + (len(JOBS) - POSTS) + n
            return c * len(JOBS) + (len(JOBS) - POSTS - ZS - POSTS) + n

        def filled(eng, c, job):
            eng.wait_ge(s_side_filled, product(c, job) + 1)

        def moved(eng, c, job):
            eng.wait_ge(s_side_moved, product(c, job) + 1)

        def side_free(eng, c, job):
            n = product(c, job)
            if not isinstance(n, int) or n > 0:
                eng.wait_ge(s_side_moved, n)

        def reached(eng, s, value):
            if not isinstance(value, int) or value > 0:
                eng.wait_ge(s, value)

        def mamba_bodies(eng, body):
            body(-1, 1, False, False, True)
            body(0, 0, False, True, True)
            with eng.Fori(1, CHUNKS - 2, 2) as c0:
                for u in range(2):
                    body(c0 + u, (1 + u) % 2, True, True, True)
            body(CHUNKS - 1, 1, True, True, False)
            body(CHUNKS, 0, True, False, False)

        def item_of(i):
            pair, w = i // PAIR, i % PAIR
            return 2 * pair + w % 2, w // 2

        ON_TENSOR = [n for n in range(DS) if n not in ON_VECTOR]

        def reads_before(n, t, owners):
            i = n // 2 * PAIR + 2 * t + n % 2
            return sum(item_of(k)[0] in owners for k in range(i))

        def read_out(eng, c, n, t):
            owners, s = (ON_VECTOR, s_part) if n in ON_VECTOR else (ON_TENSOR, s_read)
            reached(eng, s, c * len(owners) * T + reads_before(n, t, owners) + 1)

        def attention_over(eng):
            for q in range(2):
                eng.wait_ge(s_x1_out[q], 16 * TILES // 2 + 16)
                eng.wait_ge(s_xh_out[q], 16 * TILES // 2 + 16)

        FIN = 8

        def mamba_sync(sp):
            attention_over(sp)
            sp.wait_ge(s_step, 5)

            def gather(c):
                for t in range(T):
                    row = sp.value_load(order[0:1, bass.ds(c * T + t, 1)], min_val=0, max_val=STEPS - 1)
                    sp.dma_start(xg[:, t:t + 1, :], normed_seq[:, bass.ds(row, 1), :]).then_inc(s_xg, 16)

            gather(0)

            def body(c, par, post, scan, pre):
                if post:
                    for q in range(2):
                        sp.wait_ge(s_yo, (c - 1) * 2 + q + 1)
                        apart(sp)
                        sp.dma_start(ssm_out[:, bass.ds((c - 1) * T + 2 * q, 2), :], yo[:, q, :, :])\
                            .then_inc(s_y_out[q], 16)
                if pre and not (isinstance(c, int) and c + 2 >= CHUNKS):
                    filled(sp, c, "h1")
                    apart(sp)
                    gather(c + 2)

            body(-1, 1, False, False, True)
            body(0, 0, False, True, True)
            with sp.Fori(1, CHUNKS - 4, 2) as c0:
                for u in range(2):
                    body(c0 + u, (1 + u) % 2, True, True, True)
            for c in range(CHUNKS - 3, CHUNKS + 1):
                body(c, c % 2, True, c < CHUNKS, c < CHUNKS - 1)
            for q in range(2):
                sp.wait_ge(s_y_out[q], 16 * CHUNKS + 16)
            def group(g, p):
                for t in range(FIN):
                    row = sp.value_load(order[0:1, bass.ds(g * FIN + t, 1)], min_val=0, max_val=STEPS - 1)
                    sp.dma_start(fin_y[:, p, t:t + 1, :], ssm_out[:, bass.ds(row, 1), :]).then_inc(s_fin_y[p], 16)
                sp.dma_start(fin_r[:, p, :, :], resid_seq[:, bass.ds(g * FIN, FIN), :]).then_inc(s_fin_r[p], 16)

            def store(g, p):
                sp.wait_ge(s_sum, g + 1)
                sp.dma_start(out[:, bass.ds(g * FIN, FIN), :], fin_r[:, p, :, :]).then_inc(s_out, 16)

            group(0, 0)
            for g in range(STEPS // FIN):
                if g + 1 < STEPS // FIN:
                    if g >= 1:
                        sp.wait_ge(s_out, 16 * g)
                    group(g + 1, (g + 1) % 2)
                store(g, g % 2)
            sp.wait_ge(s_out, 16 * (STEPS // FIN))

        def mamba_gpsimd(gp):
            attention_over(gp)
            gp.memset(raw[:, :, 0:(TAPS - 1) * P], 0.0).then_inc(s_carried, 1)

            def make_diag(c, par, n):
                if n >= 4:
                    if n - 4 in ON_TENSOR:
                        read_out(gp, c, n - 4, T - 1)
                elif not (isinstance(c, int) and c == 0):
                    read_out(gp, c - 1, n + DS - 4, T - 1)
                if n == 0:
                    moved(gp, c - 1, "bc")
                gp.tensor_tensor(c_diag[:, n % 4, :, :], ident[:, None, :].to_broadcast([P, T, P]),
                                 bc[:, par, :, DS + n:DS + n + 1].to_broadcast([P, T, P]), ALU.mult)\
                    .then_inc(s_cdiag, 1)

            def body(c, par, post, scan, pre):
                for pair in range(DS // 2):
                    for k in range(2):
                        if pair < DS // 2 - 1 and scan and 2 * pair + 2 + k in ON_TENSOR:
                            make_diag(c, par, 2 * pair + 2 + k)
                    if pre and pair == 1:
                        gp.wait_ge(s_xg, (c + 2) * 16 * T)
                        gp.tensor_tensor(xg[:, :, :], xg[:, :, :], mod_scale[:, None, :].to_broadcast([P, T, D]),
                                         ALU.mult).then_inc(s_modulated, 1)
                        gp.wait_ge(s_modulated, (c + 1) * 2 + 1)
                        gp.tensor_tensor(xg[:, :, :], xg[:, :, :], mod_shift[:, None, :].to_broadcast([P, T, D]),
                                         ALU.add).then_inc(s_modulated, 1)
                        if not (isinstance(c, int) and c == -1):
                            gp.wait_ge(s_tap, (c + 1) * 3 * CB)
                            apart(gp)
                            gp.tensor_copy(raw[:, :, 0:(TAPS - 1) * P], raw[:, :, TOK:TOK + (TAPS - 1) * P])\
                                .then_inc(s_carried, 1)
                    if pre and pair == 7:
                        gp.wait_ge(s_dt, (c + 2) * CB)
                        gp.wait_ge(s_xs, (c + 2) * CB)
                        gp.tensor_tensor(tmp[:, :, :], dtT[:, 1 - par, :, :], xs[:, :, :], ALU.mult)\
                            .then_inc(s_dtxT, 1)
                    if pre and pair == DS // 2 - 1:
                        for k in range(2):
                            make_diag(c + 1, 1 - par, k)

            mamba_bodies(gp, body)

        def mamba_tensor(pe):
            attention_over(pe)
            pe.wait_ge(s_prep, 1)

            def turn_decay(c, i):
                n, t = item_of(i)
                pe.wait_ge(s_decay, c * ITEMS + n * CB + CB)
                before = {0: -1, 1: -3, 2: -2}.get(i, i - DECAY_BANKS)
                reached(pe, s_state, c * ITEMS + before + 1)
                for m in range(CB):
                    mm = pe.transpose(dec_bank[i % DECAY_BANKS][:, m * P:(m + 1) * P],
                                      decay[:, n % 4, m, t * P:(t + 1) * P], ident[:, :])
                mm.then_inc(s_turned, 1)

            def read_state(c, i):
                n, t = item_of(i)
                pe.wait_ge(s_state, c * ITEMS + i + 1)
                pe.wait_ge(s_cdiag, c * len(ON_TENSOR) + ON_TENSOR.index(n) + 1)
                h = state[:, n, :] if t == T - 1 else fresh[:, n % 2, t % 2, :]
                pe.matmul(y_bank[t][:, :], c_diag[:, n % 4, t, :], h, start=False, stop=(n == DS - 1),
                          skip_group_check=True).then_inc(s_read, 1)

            def skip_term(c, t):
                if t == 0:
                    pe.wait_ge(s_xs, (c + 1) * CB)
                reached(pe, s_summed, (c - 1) * T + t + 1)
                for m in range(CB):
                    mm = pe.matmul(y_bank[t][:, m * P:(m + 1) * P], xs[:, m, t * P:(t + 1) * P], d_diag[:, m, :],
                                   start=(m == 0), stop=False, skip_group_check=True)
                mm.then_inc(s_skip, 1)

            def fill(c, par, job, piece):
                pieces = len(SLOTS[job])
                if piece == 0:
                    side_free(pe, c, job)
                kind, k = (job[:-1], int(job[-1])) if job[-1].isdigit() else (job, 0)
                if kind == "turn":
                    pe.wait_ge(s_gated, (c - 1) * T + k + 1)
                    for m in range(CB):
                        mm = pe.transpose(side[:, m * P:(m + 1) * P], zs[:, k, m * P:(m + 1) * P], ident[:, :])
                elif kind == "out":
                    if piece == 0:
                        moved(pe, c, "turn1" if k == 0 else "turn3")
                    both = [(q, m) for q in range(2) for m in range(CB)]
                    for q, m in both[piece * 3:piece * 3 + 3]:
                        mm = pe.matmul(side[:, q * D:(q + 1) * D], gT[:, q, m, :], w_out[:, m, :],
                                       start=(m == 0), stop=(m == CB - 1))
                elif kind == "z":
                    mm = pe.matmul(side[:, :], hT[:, piece, k * P:(k + 1) * P], w_in[:, piece, DI:2 * DI],
                                   start=(piece == 0), stop=(piece == FB - 1))
                elif kind == "h":
                    pe.wait_ge(s_modulated, (c + 2) * 2)
                    for t in range(T):
                        mm = pe.transpose(side[:, t * P:(t + 1) * P], xg[:, t, k * P:(k + 1) * P], ident[:, :])
                elif kind == "u":
                    if piece == 0:
                        moved(pe, c, "h1")
                    mm = pe.matmul(side[:, :], w_in[:, piece, k * P:(k + 1) * P], hT[:, piece, :],
                                   start=(piece == 0), stop=(piece == FB - 1))
                elif kind == "dtr":
                    pe.wait_ge(s_xs, (c + 1) * CB + piece + 1)
                    mm = pe.matmul(side[0:DTR, :], w_xp[:, piece, 0:DTR], xs[:, piece, :],
                                   start=(piece == 0), stop=(piece == CB - 1))
                elif kind == "bc":
                    t = piece
                    for m in range(CB):
                        mm = pe.matmul(side[:, t * 2 * DS:(t + 1) * 2 * DS], xs[:, m, t * P:(t + 1) * P],
                                       w_xp[:, m, DTR:DTR + 2 * DS], start=(m == 0), stop=(m == CB - 1))
                elif kind == "dt":
                    moved(pe, c, "dtr")
                    mm = pe.matmul(side[:, :], w_dt[:, k * P:(k + 1) * P], dtrT[:, :], start=True, stop=True)
                elif kind == "x":
                    pe.wait_ge(s_dtxT, c + 2)
                    for m in range(CB):
                        mm = pe.transpose(side[:, m * P:(m + 1) * P], tmp[:, m, k * P:(k + 1) * P], ident[:, :])
                if piece == pieces - 1:
                    mm.then_inc(s_side_filled, 1)

            def body(c, par, post, scan, pre):
                for i in range(ITEMS):
                    if i + 2 < ITEMS:
                        if scan:
                            turn_decay(c, i + 2)
                    elif pre:
                        turn_decay(c + 1, i + 2 - ITEMS)
                    if scan and i in (1, 3, 5, 7):
                        skip_term(c, i // 2)
                    for n, job in enumerate(JOBS):
                        if i in SLOTS[job] and (post if n < POSTS else scan if n < POSTS + ZS else pre):
                            fill(c, par, job, SLOTS[job].index(i))
                    if scan and i >= 2 and item_of(i - 2)[0] in ON_TENSOR:
                        read_state(c, i - 2)
                if scan:
                    read_state(c, ITEMS - 2)
                    read_state(c, ITEMS - 1)

            mamba_bodies(pe, body)

        def mamba_scalar(act):
            attention_over(act)
            act.wait_ge(s_ssm_w, 16 * 6)
            act.activation(decay_rate[:, :, :], decay_rate[:, :, :], ACT.Exp).then_inc(s_prep_a, 1)
            act.wait_ge(s_prep, 1)

            def make_decay(c, par, n, m):
                reached(act, s_turned, c * ITEMS + (n // 2 - 2) * PAIR + PAIR - 1 + n % 2)
                if n == 0:
                    act.wait_ge(s_dt, c * CB + m + 1)
                act.activation(decay[:, n % 4, m, :], dtT[:, par, m, :], ACT.Exp, scale=decay_rate[:, m, n:n + 1])\
                    .then_inc(s_decay, 1)

            def move(c, par, job):
                filled(act, c, job)
                kind, k = (job[:-1], int(job[-1])) if job[-1].isdigit() else (job, 0)
                if kind == "turn":
                    if k < 2:
                        if not (isinstance(c, int) and c == 1):
                            filled(act, c - 1, "out1")
                    else:
                        filled(act, c, "out0")
                    ins = act.activation(gT[:, k % 2, :, :].rearrange("p a b -> p (a b)"), side[:, :], ACT.Copy)
                elif kind == "z":
                    ins = act.activation(zs[:, k, :], side[:, :], ACT.Copy)
                elif kind == "h":
                    ins = act.activation(hT[:, k, :], side[:, :], ACT.Copy)
                elif kind == "u":
                    if k == 0:
                        act.wait_ge(s_carried, c + 2)
                    ins = act.activation(raw[:, k, (TAPS - 1) * P:], side[:, :], ACT.Copy)
                elif kind == "dtr":
                    ins = act.activation(dtrT[:, :], side[0:DTR, :], ACT.Copy)
                elif kind == "bc":
                    ins = act.activation(bc[:, 1 - par, :, :].rearrange("p a b -> p (a b)"),
                                         side[:, 0:T * 2 * DS], ACT.Copy)
                elif kind == "dt":
                    ins = act.activation(dtT[:, 1 - par, k, :], side[:, :], ACT.Identity, bias=dt_bias[:, k:k + 1])
                elif kind == "x":
                    ins = act.activation(dtx[:, 1 - par, k, :], side[:, :], ACT.Copy)
                ins.then_inc(s_side_moved, 1)
                if kind == "u":
                    moved(act, c, job)
                    if k == 0:
                        reached(act, s_skip, (c + 1) * T)
                    act.activation(xs[:, k, :], raw[:, k, (TAPS - 1) * P:], ACT.Identity,
                                   scale=taps[:, k, TAPS - 1:TAPS], bias=conv_bias[:, k:k + 1]).then_inc(s_tap0, 1)

            flat = tmp[:, :, :].rearrange("p a b -> p (a b)")

            def body(c, par, post, scan, pre):
                for i in range(ITEMS):
                    n, m = 2 * (i // PAIR + 1) + (i % PAIR) // CB, i % CB
                    if n < DS:
                        if scan:
                            make_decay(c, par, n, m)
                    elif pre:
                        make_decay(c + 1, 1 - par, n - DS, m)
                    for k, job in enumerate(JOBS):
                        if min(SLOTS[job][-1] + 1, ITEMS - 1) == i and job[:3] != "out" and \
                                (post if k < POSTS else scan if k < POSTS + ZS else pre):
                            move(c, par, job)
                    if scan and i == 24:
                        moved(act, c, "z3")
                        act.activation(flat, zs[:, :, :].rearrange("p a b -> p (a b)"), ACT.Tanh, scale=0.5)\
                            .then_inc(s_ztanh, 1)
                    if pre and i in [TAP_SLOT + 6 + 2 * m for m in range(CB)]:
                        m = (i - TAP_SLOT - 6) // 2
                        act.wait_ge(s_tap, (c + 1) * len(TAP_ORDER) + TAP_ORDER.index((m, TAPS - 2)) + 1)
                        if m == 0:
                            reached(act, s_zs, (c + 1) * T)
                        act.activation(tmp[:, m, :], xs[:, m, :], ACT.Tanh, scale=0.5).then_inc(s_xtanh, 1)
                    if pre and i == 53:
                        v = dtT[:, 1 - par, :, :].rearrange("p a b -> p (a b)")
                        moved(act, c, "dt3")
                        act.wait_ge(s_xs, (c + 2) * CB)
                        act.activation(flat, v, ACT.Abs).then_inc(s_softexp, 1)
                        act.wait_ge(s_softexp, (c + 1) * 3 + 1)
                        act.activation(flat, flat, ACT.Exp, scale=-1.0).then_inc(s_softexp, 1)
                        act.wait_ge(s_softexp, (c + 1) * 3 + 2)
                        act.activation(flat, flat, ACT.Ln, bias=1.0).then_inc(s_softexp, 1)

            mamba_bodies(act, body)

        def mamba_vector(ve):
            attention_over(ve)
            ve.wait_ge(s_ssm_w, 16 * 6)
            ve.tensor_scalar(w_xp[:, :, 0:DTR], w_xp[:, :, 0:DTR], 0.5, None, ALU.mult).then_inc(s_step, 1)
            ve.tensor_scalar(w_xp[:, :, DTR:DTR + DS], w_xp[:, :, DTR:DTR + DS], 0.25, None, ALU.mult)\
                .then_inc(s_step, 1)
            ve.tensor_scalar(w_xp[:, :, DTR + DS:], w_xp[:, :, DTR + DS:], 0.5, None, ALU.mult).then_inc(s_step, 1)
            for m in range(CB):
                ve.tensor_scalar(d_diag[:, m, :], ident[:, :], d_col[:, m:m + 1], 0.5, ALU.mult, ALU.mult)\
                    .then_inc(s_step, 1)
            ve.wait_ge(s_prep_a, 1)
            ve.tensor_scalar(decay_rate[:, :, :], decay_rate[:, :, :], -1.0, None, ALU.mult).then_inc(s_step, 1)
            ve.memset(state[:, :, :], 0.0).then_inc(s_step, 1)
            ve.wait_ge(s_step, 19 + 9)
            ve.sem_inc(s_prep, 1)

            def keep_state(c, i):
                n, t = item_of(i)
                h = state[:, n, :] if t == 0 else fresh[:, n % 2, (t - 1) % 2, :]
                ve.wait_ge(s_turned, c * ITEMS + i + 1)
                reached(ve, s_state, c * ITEMS + i - 1)
                ve.tensor_tensor(dec_bank[i % DECAY_BANKS][:, :], dec_bank[i % DECAY_BANKS][:, :], h, ALU.mult)\
                    .then_inc(s_kept, 1)

            def feed_state(c, par, i):
                n, t = item_of(i)
                h = state[:, n, :] if t == T - 1 else fresh[:, n % 2, t % 2, :]
                if i < PAIR and i % 2 == 0:
                    moved(ve, c - 1, f"x{t}")
                ve.wait_ge(s_kept, c * ITEMS + i + 1)
                if t == 2:
                    read_out(ve, c, n, 0)
                elif t < 2 and n >= 2:
                    read_out(ve, c, n - 2, 2 - t)
                elif t < 2 and not (isinstance(c, int) and c == 0):
                    read_out(ve, c - 1, n + DS - 2, 2 - t)
                ve.scalar_tensor_tensor(h, dtx[:, par, t, :], bc[:, par, t, n:n + 1], dec_bank[i % DECAY_BANKS][:, :],
                                        ALU.mult, ALU.add).then_inc(s_state, 1)

            def read_part(c, par, i):
                n, t = item_of(i)
                h = state[:, n, :] if t == T - 1 else fresh[:, n % 2, t % 2, :]
                coef = bc[:, par, t, DS + n:DS + n + 1]
                ve.wait_ge(s_state, c * ITEMS + i + 1)
                if n == ON_VECTOR[0]:
                    ins = ve.tensor_scalar(part[:, t, :], h, coef, None, ALU.mult)
                else:
                    ve.wait_ge(s_part, c * len(ON_VECTOR) * T + reads_before(n, t, ON_VECTOR) - T + 1)
                    ins = ve.scalar_tensor_tensor(part[:, t, :], h, coef, part[:, t, :], ALU.mult, ALU.add)
                ins.then_inc(s_part, 1)

            def rows(c, q):
                filled(ve, c, f"out{q}")
                ve.wait_ge(s_y_out[q], c * 16)
                ve.tensor_tensor(yo[:, q, :, :], side[:, :].rearrange("p (a b) -> p a b", b=D),
                                 mod_gate[:, None, :].to_broadcast([P, 2, D]), ALU.mult).then_inc(s_side_moved, 1)
                moved(ve, c, f"out{q}")
                ve.sem_inc(s_yo, 1)

            def body(c, par, post, scan, pre):
                if post:
                    ve.wait_ge(s_read, c * len(ON_TENSOR) * T)
                    ve.wait_ge(s_part, c * len(ON_VECTOR) * T)
                    ve.wait_ge(s_zs, c * T)
                for i in range(0, ITEMS, 2):
                    if post and i < 2 * T:
                        t = i // 2
                        ve.tensor_tensor(part[:, t, :], y_bank[t][:, :], part[:, t, :], ALU.add).then_inc(s_summed, 1)
                    if scan:
                        keep_state(c, i)
                        keep_state(c, i + 1)
                    if post and i < 2 * T:
                        ve.wait_ge(s_summed, (c - 1) * T + t + 1)
                        ve.tensor_tensor(zs[:, t, :], part[:, t, :], zs[:, t, :], ALU.mult).then_inc(s_gated, 1)
                    if scan:
                        feed_state(c, par, i)
                        feed_state(c, par, i + 1)
                        for k in (i - 2, i - 1):
                            if k >= 0 and item_of(k)[0] in ON_VECTOR:
                                read_part(c, par, k)
                    if post and i == 6:
                        rows(c, 0)
                    if post and i == 14:
                        rows(c, 1)
                    if scan and 26 <= i < 26 + 2 * T:
                        t = (i - 26) // 2
                        ve.wait_ge(s_ztanh, c + 1)
                        ve.scalar_tensor_tensor(zs[:, t, :], tmp[:, t, :], 1.0, zs[:, t, :], ALU.add, ALU.mult)\
                            .then_inc(s_zs, 1)
                    for at, (m, k) in enumerate(TAP_ORDER):
                        if pre and i == TAP_SLOT + 2 * (m + k):
                            ve.wait_ge(s_tap0, (c + 1) * CB + m + 1)
                            if k:
                                ve.wait_ge(s_tap, (c + 1) * len(TAP_ORDER) + TAP_ORDER.index((m, k - 1)) + 1)
                            ve.scalar_tensor_tensor(xs[:, m, :], raw[:, m, k * P:k * P + TOK], taps[:, m, k:k + 1],
                                                    xs[:, m, :], ALU.mult, ALU.add).then_inc(s_tap, 1)
                    if pre and TAP_SLOT + 8 <= i < TAP_SLOT + 8 + 2 * CB:
                        m = (i - TAP_SLOT - 8) // 2
                        ve.wait_ge(s_xtanh, (c + 1) * CB + m + 1)
                        ve.scalar_tensor_tensor(xs[:, m, :], tmp[:, m, :], 1.0, xs[:, m, :], ALU.add, ALU.mult)\
                            .then_inc(s_xs, 1)
                    if pre and i == 54:
                        ve.wait_ge(s_softexp, (c + 2) * 3)
                        for m in range(CB):
                            v = dtT[:, 1 - par, m, :]
                            ve.scalar_tensor_tensor(v, v, 0.0, tmp[:, m, :], ALU.max, ALU.add).then_inc(s_dt, 1)

            mamba_bodies(ve, body)
            for g in range(STEPS // FIN):
                p = g % 2
                ve.wait_ge(s_fin_r[p], 16 * (g // 2 + 1))
                ve.wait_ge(s_fin_y[p], 16 * FIN * (g // 2 + 1))
                ve.tensor_tensor(fin_r[:, p, :, :], fin_r[:, p, :, :], fin_y[:, p, :, :], ALU.add).then_inc(s_sum, 1)

        @block.sync
        def _(sp):
            with nc.allow_non_contiguous_dma(reason="short per-feature vectors"):
                for dst, src in ((ns_col, norm_scale), (nb_col, norm_bias), (bk_col, bk),
                                 (fns_col, film_norm_scale), (fnb_col, film_norm_bias), (fb_col, film_b),
                                 (conv_bias, conv_b), (dt_bias, b_dt), (d_col, D_param)):
                    sp.dma_start(dst, src.rearrange("(c p) -> p c", p=P)).then_inc(s_cols, 16)
            sp.dma_start(cond_s[:, :], cond).then_inc(s_cond, 16)
            sp.dma_start(film_w[:, :, :], film_W.rearrange("(c p) n -> p c n", p=P)).then_inc(s_cond, 16)
            sp.dma_start(ada_w[:, :, :], W_ada.rearrange("(c p) n -> p c n", p=P)).then_inc(s_cond, 16)
            sp.dma_start(b_mod[:, :], b_ada.rearrange("(a n) -> a n", a=1)).then_inc(s_cond, 16)
            sp.dma_start(gamma_bc[:, :], gamma.rearrange("(a n) -> a n", a=1).to_broadcast([P, D])).then_inc(s_cond, 16)
            sp.dma_start(beta_bc[:, :], beta.rearrange("(a n) -> a n", a=1).to_broadcast([P, D])).then_inc(s_cond, 16)
            sp.dma_start(mask_i[:, :], mask_flat.rearrange("(k p) -> k p", p=P)).then_inc(s_cond, 16)
            sp.dma_start(order_i[:, :], itok.rearrange("(a n) -> a n", a=1)).then_inc(s_cond, 16)
            for dst, src in ((w_qv[:, :, 0:D], Wq), (w_qv[:, :, D:2 * D], Wv), (w_k[:, :, :], Wk),
                             (w_fo[:, :, :], film_out_W)):
                sp.dma_start(dst, src.rearrange("(c p) n -> p c n", p=P)).then_inc(s_attn_w, 16)
            for dst, src in ((b_qv[:, 0:D], bq), (b_qv[:, D:2 * D], bv), (b_fo[:, :], film_out_b)):
                sp.dma_start(dst, src.rearrange("(a n) -> a n", a=1)).then_inc(s_attn_w, 16)

            def iteration(j, u, stages):
                if 0 in stages:
                    reuse(sp, S["x1_ready"], j, XRING)
                    apart(sp)
                    sp.dma_start(xt[:, u, :], x_tok[bass.ts(j, P), :]).then_inc(s_x[u], 16)
                    reuse(sp, S["mneg_ready"], j, 2)
                    apart(sp)
                    sp.dma_start(mask_bc[:, u % 2, :],
                                 mask_flat[bass.ts(j, P)].rearrange("(a n) -> a n", a=1).to_broadcast([P, P]))\
                        .then_inc(s_mk[u % 2], 16)
                if 4 in stages:
                    k, p = j - 4, u % 2
                    later(sp, S["x1_ready"], k)
                    apart(sp)
                    sp.dma_start(resid[bass.ts(k, P), :], x1[:, p, :]).then_inc(s_x1_out[p], 16)
                    later(sp, S["xh_ready"], k)
                    apart(sp)
                    sp.dma_start(normed[bass.ts(k, P), :], xh[:, p, :]).then_inc(s_xh_out[p], 16)
                if isinstance(j, int) and j == 3:
                    for dst, src in ((w_in[:, :, :], W_in), (w_xp[:, :, :], W_xp), (w_out[:, :, :], W_out)):
                        sp.dma_start(dst, src.rearrange("(c p) n -> p c n", p=P)).then_inc(s_ssm_w, 16)
                    sp.dma_start(w_dt[:, :], W_dt).then_inc(s_ssm_w, 16)
                    sp.dma_start(decay_rate[:, :, :], A_log.rearrange("(c p) n -> p c n", p=P)).then_inc(s_ssm_w, 16)
                    sp.dma_start(taps[:, :, :], conv_w.rearrange("(c p) o k -> p c (o k)", p=P)).then_inc(s_ssm_w, 16)

            attention_iterations(sp, iteration)
            mamba_sync(sp)

        @block.gpsimd
        def _(gp):
            gp.memset(ident[:, :], 0.0).then_inc(s_pool, 1)
            gp.memset(head_mask[:, :, :], 1.0).then_inc(s_pool, 1)
            gp.memset(half_pow[:, :], -0.5).then_inc(s_pool, 1)
            gp.memset(ones_row[:, :], 1.0).then_inc(s_pool, 1)
            gp.wait_ge(s_pool, 4)
            gp.affine_select(out=ident[:, :], in_=ident[:, :], compare_op=ALU.not_equal, fill=1.0, base=0,
                             pattern=[[-1, P]], channel_multiplier=1).then_inc(s_pool, 1)
            hm = head_mask[:, :, :].rearrange("p a (g c) -> p a g c", c=DH)
            gp.affine_select(out=hm, in_=hm, compare_op=ALU.is_ge, fill=0.0, base=0,
                             pattern=[[0, 4], [-DH, P // DH], [0, DH]], channel_multiplier=1).then_inc(s_pool, 1)
            gp.wait_ge(s_pool, 6)
            gp.affine_select(out=hm, in_=hm, compare_op=ALU.is_ge, fill=0.0, base=DH - 1,
                             pattern=[[0, 4], [DH, P // DH], [0, DH]], channel_multiplier=-1).then_inc(s_pool, 1)
            gp.wait_ge(s_pool, 7)

            def rsqrt(norm, slot, tile, meanvar, plus, done):
                later(gp, S[meanvar], tile)
                apart(gp)
                gp.tensor_scalar(rstd[:, norm, slot, 1:2], mv[:, norm, slot, 1:2], EPS, None, ALU.add)\
                    .then_inc(S[plus], 1)
                later(gp, S[plus], tile)
                gp.tensor_tensor(rstd[:, norm, slot, 0:1], rstd[:, norm, slot, 1:2], half_pow[:, :], ALU.pow)\
                    .then_inc(S[done], 1)

            def iteration(j, u, stages):
                if 0 in stages:
                    rsqrt(0, u % 2, j, "x_meanvar", "x_plus", "x_rstd")
                if 2 in stages:
                    rsqrt(1, u % 2, j - 2, "y_meanvar", "y_plus", "y_rstd")
                if 3 in stages:
                    rsqrt(2, (u + 1) % 2, j - 3, "x1_meanvar", "x1_plus", "x1_rstd")

            attention_iterations(gp, iteration)
            mamba_gpsimd(gp)

        @block.tensor
        def _(pe):
            pe.wait_ge(s_pool, 7)
            pe.wait_ge(s_ve, 1)
            for c in range(KC):
                mm = pe.transpose(bank[0][:, c * P:(c + 1) * P], cond_s[:, c * P:(c + 1) * P], ident[:, :])
            mm.then_inc(s_pe, 1)
            pe.wait_ge(s_ve, 2)
            pe.transpose(bank[1][:, 0:TILES], mask_f[:, :], ident[0:STEPS, 0:STEPS]).then_inc(s_pe, 1)
            pe.wait_ge(s_ae, 2)
            for m in range(4):
                for c in range(KC):
                    mm = pe.matmul(bank[2][:, m * P:(m + 1) * P], film_w[:, c, m * P:(m + 1) * P], cond_T[:, c, :],
                                   start=(c == 0), stop=(c == KC - 1))
            mm.then_inc(s_pe, 1)
            for dst, a, b in ((bank[3], 0, 2 * D), (bank[4], 2 * D, 3 * D)):
                pe.matmul(dst[:, 0:b - a], ones_row[:, :], b_mod[:, a:b], start=True, stop=False)
                for c in range(KC):
                    mm = pe.matmul(dst[:, 0:b - a], cond_T[:, c, :], ada_w[:, c, a:b], start=False,
                                   stop=(c == KC - 1))
            mm.then_inc(s_pe, 1)
            pe.wait_ge(s_attn_w, 16 * 7)
            pe.wait_ge(s_const, 1)

            def heads_product(p, q):
                rows = slice(q * STEPS, (q + 1) * STEPS)
                for h in range(FB):
                    mm = pe.matmul(b_at[:, (q * FB + h) * P:(q * FB + h + 1) * P], vt[rows, p, h * P:(h + 1) * P],
                                   kq[rows, p, h * P:(h + 1) * P], start=True, stop=True)
                return mm

            def iteration(j, u, stages):
                p1, p2 = (u - 1) % 2, (u - 2) % 2
                if 2 in stages:
                    k = j - 2
                    later(pe, S["kq_ready"], k)
                    later(pe, S["v_ready"], k)
                    reuse(pe, S["at_masked"], k, 1)
                    heads_product(p2, 0).then_inc(S["at_half"], 1)
                if 1 in stages:
                    k = j - 1
                    later(pe, S["xnT_ready"], k)
                    reuse(pe, S["k_biased"], k, 1)
                    for m in range(FB):
                        for c in range(FB):
                            mm = pe.matmul(b_kT[:, m * P:(m + 1) * P], w_k[:, c, m * P:(m + 1) * P],
                                           xnT[:, p1, c, :], start=(c == 0), stop=(c == FB - 1))
                    mm.then_inc(S["kT_ready"], 1)
                if 2 in stages:
                    later(pe, S["at_half"], j - 2)
                    heads_product(p2, 1).then_inc(S["at_ready"], 1)
                if 1 in stages:
                    k = j - 1
                    reuse(pe, S["v_ready"], k, 1)
                    pe.matmul(b_qvp[:, :], ones_row[:, :], b_qv[:, :], start=True, stop=False)
                    for c in range(FB):
                        mm = pe.matmul(b_qvp[:, :], xnT[:, p1, c, :], w_qv[:, c, :], start=False, stop=(c == FB - 1))
                    mm.then_inc(S["qv_ready"], 1)
                if 2 in stages:
                    k = j - 2
                    later(pe, S["at_masked"], k)
                    reuse(pe, S["y_scaled"], k, 1)
                    for i in range(4):
                        q, h = i // FB, i % FB
                        mm = pe.matmul(b_y[q * STEPS:(q + 1) * STEPS, h * P:(h + 1) * P],
                                       kq[:, p2, D + h * P + q * STEPS:D + h * P + (q + 1) * STEPS],
                                       attnT[:, i, :], start=True, stop=True)
                    mm.then_inc(S["y_ready"], 1)
                if 0 in stages:
                    later(pe, S["x_norm"], j)
                    reuse(pe, S["xnT_ready"], j, 1)
                    for c in range(FB):
                        mm = pe.transpose(b_xT[:, c * P:(c + 1) * P], xn[:, c * P:(c + 1) * P], ident[:, :])
                    mm.then_inc(S["xT_ready"], 1)
                if 3 in stages:
                    k = j - 3
                    later(pe, S["film_act"], k)
                    reuse(pe, S["x1_ready"], k, 1)
                    pe.matmul(b_fo_ps[:, 0:D], ones_row[:, :], b_fo[:, :], start=True, stop=False)
                    for c in range(FB):
                        mm = pe.matmul(b_fo_ps[:, 0:D], fs[:, c, :], w_fo[:, c, :], start=False, stop=(c == FB - 1))
                    mm.then_inc(S["proj_ready"], 1)
                if 1 in stages:
                    k = j - 1
                    later(pe, S["k_normed"], k)
                    later(pe, S["q_exp"], k)
                    reuse(pe, S["kq_ready"], k, 1)
                    for c in range(FB):
                        pe.transpose(b_kq[:, c * P:(c + 1) * P],
                                     kT[:, p1, c * SEQS:(c + 1) * SEQS, :].rearrange("p a b -> p (a b)"), ident[:, :])
                    for c in range(FB):
                        mm = pe.transpose(b_kq[:, D + c * P:D + (c + 1) * P], qe[:, p1, c * P:(c + 1) * P], ident[:, :])
                    mm.then_inc(S["kq_turned"], 1)
                if 2 in stages:
                    k = j - 2
                    later(pe, S["y_norm"], k)
                    reuse(pe, S["film_in"], k, 1)
                    for c in range(FB):
                        mm = pe.transpose(b_ynT[:, c * P:(c + 1) * P], yn[:, c * P:(c + 1) * P], ident[:, :])
                    mm.then_inc(S["ynT_ready"], 1)

            attention_iterations(pe, iteration)
            mamba_tensor(pe)

        @block.scalar
        def _(act):
            act.wait_ge(s_cond, 16 * 8)
            act.activation(cond_t[:, :], cond_s[:, :], ACT.Tanh, scale=0.5).then_inc(s_ae, 1)
            act.wait_ge(s_pe, 1)
            act.activation(cond_T[:, :, :].rearrange("p a b -> p (a b)"), bank[0][:, :], ACT.Copy).then_inc(s_ae, 1)

            def iteration(j, u, stages):
                p0, p1 = u % 2, (u - 1) % 2
                if 3 in stages:
                    later(act, S["film_in"], j - 3)
                    reuse(act, S["film_act"], j - 3, 1)
                    act.activation(fth[:, :], fu[:, :], ACT.Tanh, scale=0.5).then_inc(S["film_tanh"], 1)
                if 1 in stages:
                    k = j - 1
                    later(act, S["k_shifted"], k)
                    kk = kT[:, p1, :, :].rearrange("p a b -> p (a b)")
                    act.activation(kk, kk, ACT.Exp).then_inc(S["k_exp"], 1)
                    later(act, S["q_shifted"], k)
                    act.activation(qe[:, p1, :], qe[:, p1, :], ACT.Exp).then_inc(S["q_exp"], 1)
                    reuse(act, S["at_ready"], k, 2)
                    act.activation(vt[:, p1, :], b_qvp[:, D:2 * D], ACT.Copy, scale=keep[:, bass.ds(k, 1)])\
                        .then_inc(S["v_ready"], 1)
                if 0 in stages:
                    later(act, S["xT_ready"], j)
                    reuse(act, S["qv_ready"], j, 2)
                    for c in range(FB):
                        ins = act.activation(xnT[:, p0, c, :], b_xT[:, c * P:(c + 1) * P], ACT.Identity,
                                             scale=ns_col[:, c:c + 1], bias=nb_col[:, c:c + 1])
                    ins.then_inc(S["xnT_ready"], 1)
                if 1 in stages:
                    k = j - 1
                    later(act, S["kq_turned"], k)
                    reuse(act, S["y_ready"], k, 2)
                    act.activation(kq[:, p1, :], b_kq[:, :], ACT.Copy).then_inc(S["kq_ready"], 1)

            act.wait_ge(s_const, 1)
            attention_iterations(act, iteration)
            mamba_scalar(act)

        @block.vector
        def _(ve):
            for q in range(2):
                for stored in (s_x1_out[q], s_xh_out[q], s_y_out[q]):
                    ve.sem_inc(stored, 16)
            ve.wait_ge(s_ae, 1)
            ve.scalar_tensor_tensor(cond_t[:, :], cond_t[:, :], 1.0, cond_s[:, :], ALU.add, ALU.mult)\
                .then_inc(s_step, 1)
            ve.wait_ge(s_step, 1)
            ve.tensor_scalar(cond_s[:, :], cond_t[:, :], 0.5, None, ALU.mult).then_inc(s_ve, 1)
            ve.tensor_scalar(mask_f[:, :], mask_i[:, :], 1.0, None, ALU.not_equal).then_inc(s_ve, 1)
            ve.tensor_copy(order_f[:, 0, :], order_i[:, :]).then_inc(s_step, 1)
            ve.wait_ge(s_step, 2)
            ve.tensor_scalar(order_f[:, 1, :], order_f[:, 0, :], 0.0, float(STEPS), ALU.is_lt, ALU.mult)\
                .then_inc(s_step, 1)
            ve.wait_ge(s_step, 3)
            ve.tensor_tensor(order_f[:, 0, :], order_f[:, 0, :], order_f[:, 1, :], ALU.add).then_inc(s_step, 1)
            ve.wait_ge(s_step, 4)
            ve.tensor_scalar(order[:, :], order_f[:, 0, :], 0.0, float(STEPS - 1), ALU.max, ALU.min)\
                .then_inc(s_step, 1)
            ve.wait_ge(s_pe, 2)
            ve.tensor_copy(keep[:, :], bank[1][:, 0:TILES]).then_inc(s_step, 1)
            ve.wait_ge(s_pe, 3)
            ve.wait_ge(s_cols, 16 * 9)
            for c in range(FB):
                ve.tensor_scalar(film_s[:, c, :], bank[2][:, c * P:(c + 1) * P], fb_col[:, c:c + 1], 1.0,
                                 ALU.add, ALU.add).then_inc(s_step, 1)
                ve.tensor_scalar(film_t[:, c, :], bank[2][:, (2 + c) * P:(3 + c) * P], fb_col[:, 2 + c:3 + c], None,
                                 ALU.add).then_inc(s_step, 1)
            ve.wait_ge(s_step, 10)
            for c in range(FB):
                ve.scalar_tensor_tensor(film_t[:, c, :], film_s[:, c, :], fnb_col[:, c:c + 1], film_t[:, c, :],
                                        ALU.mult, ALU.add).then_inc(s_step, 1)
            ve.wait_ge(s_step, 12)
            for c in range(FB):
                ve.tensor_scalar(film_s[:, c, :], film_s[:, c, :], fns_col[:, c:c + 1], None, ALU.mult)\
                    .then_inc(s_step, 1)
            ve.wait_ge(s_pe, 4)
            ve.scalar_tensor_tensor(mod_scale[:, :], bank[3][:, D:2 * D], 1.0, gamma_bc[:, :], ALU.add, ALU.mult)\
                .then_inc(s_step, 1)
            ve.scalar_tensor_tensor(mod_shift[:, :], bank[3][:, D:2 * D], 1.0, beta_bc[:, :], ALU.add, ALU.mult)\
                .then_inc(s_step, 1)
            ve.tensor_scalar(mod_gate[:, :], bank[4][:, 0:D], 0.5, None, ALU.mult).then_inc(s_step, 1)
            ve.wait_ge(s_step, 17)
            ve.tensor_tensor(mod_shift[:, :], bank[3][:, 0:D], mod_shift[:, :], ALU.add).then_inc(s_step, 1)
            ve.wait_ge(s_attn_w, 16 * 7)
            ve.tensor_scalar(w_fo[:, :, :], w_fo[:, :, :], 0.5, None, ALU.mult).then_inc(s_step, 1)
            ve.wait_ge(s_step, 19)
            ve.wait_ge(s_pool, 7)
            ve.sem_inc(s_const, 1)

            def norm(src, slot, p, tile, stats_done, meanvar_done):
                ve.bn_stats(stats[:, slot, :], src).then_inc(S[stats_done], 1)
                later(ve, S[stats_done], tile)
                apart(ve)
                ve.bn_aggr(mv[:, slot, p, :], stats[:, slot, :]).then_inc(S[meanvar_done], 1)

            def iteration(j, u, stages):
                p0, p1, p2, p3 = u % 2, (u - 1) % 2, (u - 2) % 2, (u - 3) % 2
                j1, j2, j3, j4 = j - 1, j - 2, j - 3, j - 4
                if 4 in stages:
                    later(ve, S["x1_rstd"], j4)
                    ve.wait_ge(s_xh_out[p0], (j4 - p0) * 8 + 16)
                    ve.tensor_scalar(xh[:, p0, :], x1[:, p0, :], mv[:, 2, p0, 0:1], rstd[:, 2, p0, 0:1],
                                     ALU.subtract, ALU.mult).then_inc(S["xh_ready"], 1)
                if 0 in stages:
                    ve.wait_ge(s_x[u], (j - u) * 4 + 16)
                    norm(xt[:, u, :], 0, p0, j, "x_stats", "x_meanvar")
                if 3 in stages:
                    later(ve, S["ynT_ready"], j3)
                    reuse(ve, S["film_act"], j3, 1)
                    for c in range(FB):
                        for q in range(SEQS):
                            a = c * P + q * STEPS
                            ins = ve.tensor_scalar(fu[:, a:a + STEPS], b_ynT[:, a:a + STEPS],
                                                   film_s[:, c, bass.ds(j3 * SEQS + q, 1)],
                                                   film_t[:, c, bass.ds(j3 * SEQS + q, 1)], ALU.mult, ALU.add)
                    ins.then_inc(S["film_in"], 1)
                if 1 in stages:
                    kk = kT[:, p1, :, :]
                    later(ve, S["kT_ready"], j1)
                    reuse(ve, S["kq_turned"], j1, 2)
                    for c in range(FB):
                        ins = ve.scalar_tensor_tensor(kk[:, c * SEQS:(c + 1) * SEQS, :].rearrange("p a b -> p (a b)"),
                                                      b_kT[:, c * P:(c + 1) * P], bk_col[:, c:c + 1], mneg[:, p1, :],
                                                      ALU.add, ALU.add)
                    ins.then_inc(S["k_biased"], 1)
                    later(ve, S["k_biased"], j1)
                    ve.tensor_reduce(kmax[:, :], kk, AX.X, ALU.max).then_inc(S["k_max"], 1)
                    later(ve, S["k_max"], j1)
                    ve.tensor_tensor(kk, kk, kmax[:, :, None].to_broadcast([P, FB * SEQS, STEPS]), ALU.subtract)\
                        .then_inc(S["k_shifted"], 1)
                if 2 in stages:
                    later(ve, S["at_ready"], j2)
                    reuse(ve, S["y_ready"], j2, 1)
                    ve.tensor_tensor(attnT[:, :, :].rearrange("p a b -> p (a b)"), b_at[:, :],
                                     head_mask[:, :, :].rearrange("p a b -> p (a b)"), ALU.mult)\
                        .then_inc(S["at_masked"], 1)
                if 0 in stages:
                    later(ve, S["x_rstd"], j)
                    reuse(ve, S["xT_ready"], j, 1)
                    ve.tensor_scalar(xn[:, :], xt[:, u, :], mv[:, 0, p0, 0:1], rstd[:, 0, p0, 0:1],
                                     ALU.subtract, ALU.mult).then_inc(S["x_norm"], 1)
                    ve.wait_ge(s_mk[p0], (j - p0) * 8 + 16)
                    ve.tensor_scalar(mneg[:, p0, :], mask_bc[:, p0, :], 1.0, -1e30, ALU.is_equal, ALU.mult)\
                        .then_inc(S["mneg_ready"], 1)
                if 3 in stages:
                    later(ve, S["film_tanh"], j3)
                    reuse(ve, S["proj_ready"], j3, 1)
                    ve.scalar_tensor_tensor(fs[:, :, :].rearrange("p a b -> p (a b)"), fth[:, :], 1.0, fu[:, :],
                                            ALU.add, ALU.mult).then_inc(S["film_act"], 1)
                if 1 in stages:
                    later(ve, S["qv_ready"], j1)
                    qps = b_qvp[:, 0:D].rearrange("p (h e) -> p h e", e=DH)
                    ve.tensor_reduce(qmax[:, :], qps, AX.X, ALU.max).then_inc(S["q_max"], 1)
                    later(ve, S["q_max"], j1)
                    ve.tensor_tensor(qe[:, p1, :].rearrange("p (h e) -> p h e", e=DH), qps,
                                     qmax[:, :, None].to_broadcast([P, HEADS, DH]), ALU.subtract)\
                        .then_inc(S["q_shifted"], 1)
                if 2 in stages:
                    later(ve, S["y_ready"], j2)
                    ve.tensor_tensor(yt[:, :].rearrange("p (h e) -> p h e", e=DH),
                                     b_y[:, 0:D].rearrange("p (h e) -> p h e", e=DH),
                                     qrec[:, (u - 2) % 4, :, None].to_broadcast([P, HEADS, DH]), ALU.mult)\
                        .then_inc(S["y_scaled"], 1)
                    later(ve, S["y_scaled"], j2)
                    norm(yt[:, :], 1, p2, j2, "y_stats", "y_meanvar")
                if 1 in stages:
                    later(ve, S["k_exp"], j1)
                    ve.tensor_reduce(ksum[:, :], kk, AX.X, ALU.add).then_inc(S["k_sum"], 1)
                    later(ve, S["q_exp"], j1)
                    ve.tensor_reduce(qsum[:, :], qe[:, p1, :].rearrange("p (h e) -> p h e", e=DH), AX.X, ALU.add)\
                        .then_inc(S["q_sum"], 1)
                    later(ve, S["k_sum"], j1)
                    ve.reciprocal(krec[:, :], ksum[:, :]).then_inc(S["k_rec"], 1)
                    later(ve, S["q_sum"], j1)
                    ve.reciprocal(qrec[:, (u - 1) % 4, :], qsum[:, :]).then_inc(S["q_rec"], 1)
                    later(ve, S["k_rec"], j1)
                    ve.tensor_tensor(kk, kk, krec[:, :, None].to_broadcast([P, FB * SEQS, STEPS]), ALU.mult)\
                        .then_inc(S["k_normed"], 1)
                if 2 in stages:
                    later(ve, S["y_rstd"], j2)
                    reuse(ve, S["ynT_ready"], j2, 1)
                    ve.tensor_scalar(yn[:, :], yt[:, :], mv[:, 1, p2, 0:1], rstd[:, 1, p2, 0:1],
                                     ALU.subtract, ALU.mult).then_inc(S["y_norm"], 1)
                if 3 in stages:
                    later(ve, S["proj_ready"], j3)
                    ve.wait_ge(s_x1_out[p3], (j3 - p3) * 8 + 16)
                    ve.tensor_tensor(x1[:, p3, :], b_fo_ps[:, 0:D], xt[:, (u - 3) % 4, :], ALU.add)\
                        .then_inc(S["x1_ready"], 1)
                    later(ve, S["x1_ready"], j3)
                    norm(x1[:, p3, :], 2, p3, j3, "x1_stats", "x1_meanvar")

            attention_iterations(ve, iteration)
            mamba_vector(ve)


_INS = ['x', 'cond_2048', 'itok_S_0_1023', 'mask_BxS_ik0', 'L0_cond_norm_scale', 'L0_cond_norm_bias',
        'L0_cond_Wq', 'L0_cond_bq', 'L0_cond_Wk', 'L0_cond_bk', 'L0_cond_Wv', 'L0_cond_bv',
        'L0_cond_film_emb_W', 'L0_cond_film_emb_b', 'L0_cond_film_norm_scale', 'L0_cond_film_norm_bias',
        'L0_cond_film_out_W', 'L0_cond_film_out_b', 'L1_cond_W_ada', 'L1_cond_b_ada', 'L1_cond_gamma',
        'L1_cond_beta', 'L1_cond_W_in', 'L1_cond_conv_w', 'L1_cond_conv_b', 'L1_cond_W_xp', 'L1_cond_W_dt',
        'L1_cond_b_dt', 'L1_cond_A_log', 'L1_cond_D_param', 'L1_cond_W_out']
_OUTS = [((BATCH, STEPS, D), 'float32')]


def kernel(**inputs):
    import numpy as _np
    import concourse.bacc as _bacc
    from concourse import mybir as _mybir
    from concourse.bass_utils import run_bass_kernel_spmd as _run

    nc = _bacc.Bacc("TRN2", target_bir_lowering=False, num_devices=1)
    arrays, args = {}, []
    for name in _INS:
        a = _np.ascontiguousarray(inputs[name])
        arrays[f"in_{name}_dram"] = a
        args.append(nc.dram_tensor(f"in_{name}_dram", a.shape, _mybir.dt.from_np(a.dtype), kind="ExternalInput").ap())
    for i, (shape, dtype) in enumerate(_OUTS):
        dt = _mybir.dt.from_np(_np.dtype(dtype))
        args.append(nc.dram_tensor(f"out_{i}_dram", shape, dt, kind="ExternalOutput").ap())
    build(nc, *args)
    r = _run(nc, [arrays], core_ids=[0])
    got = tuple(r.results[0][f"out_{i}_dram"] for i in range(len(_OUTS)))
    return got[0]
```
